# Optimizing a Trainium2 kernel written in Bass

```python
import numpy as np
import jax
import jax.numpy as jnp

def _softmax(x, axis=-1):
    return jax.nn.softmax(x, axis=axis)

def _gelu(x):
    return jax.nn.gelu(x, approximate=True)

def _silu(x):
    return jax.nn.silu(x)

def _sigmoid(x):
    return jax.nn.sigmoid(x)

def _layernorm(x, axis=-1, eps=1e-05):
    m = jnp.mean(x, axis=axis, keepdims=True)
    v = jnp.var(x, axis=axis, keepdims=True)
    return (x - m) / jnp.sqrt(v + eps)

def _scatter_add(tgt, idx, src, axis=0):
    return tgt.at[idx].add(src)

def _segment_sum(src, seg, n):
    return jax.ops.segment_sum(src, seg, n)
kernel_name = 'mk_prb_d1_jaxref_r4_7df91a'

def setup_inputs(seed: int=0):
    np.random.seed(seed)
    _w = jnp.asarray

    def _L0_attn_setup():
        import math
        import jax, jax.numpy as jnp
        import numpy as np
        IN_F, OUT_F, HID = (1024, 1024, 1024)
        WINDOW, STRIPES = (6, 3)

        def make_sparse_mask(n_in=IN_F, n_out=OUT_F, window=WINDOW, stripes=STRIPES):
            m = np.zeros((n_in, n_out), dtype=np.float32)
            stride = int(math.sqrt(n_in))
            for k in range(stripes):
                ps = stride * k
                for i in range(0, n_in, window):
                    m[ps + i:ps + i + window, i:i + window] = 1.0
            mb = m.astype(bool)
            return jnp.asarray((mb | mb.T).astype(np.float32))
        key = jax.random.key(seed)
        k1, k2, k3, k4 = jax.random.split(key, 4)
        scale = 1.0 / math.sqrt(IN_F)
        x = jax.random.normal(k1, (8, 192, IN_F), dtype=jnp.float32)
        w1 = jax.random.normal(k2, (HID, IN_F), dtype=jnp.float32) * scale
        w2 = jax.random.normal(k3, (OUT_F, HID), dtype=jnp.float32) * scale
        b2 = jax.random.normal(k4, (OUT_F,), dtype=jnp.float32) * scale
        return {'x': x, 'w1': w1, 'w2': w2, 'b2': b2, 'sparse_mask': make_sparse_mask()}
    _L0_attn_in = _L0_attn_setup()

    def _L0_ffn_setup():
        import jax, jax.numpy as jnp
        import numpy as np
        E4M3_MAX = 448.0
        E5M2_MAX = 57344.0
        EPS = 1e-12
        IN_FEATURES = 1024
        OUT_FEATURES = 1024
        BATCH, SEQ = (1, 512)

        def _amax_to_scale(amax, fp8_max):
            return fp8_max / jnp.maximum(amax, EPS)

        def _to_fp8_saturated(t, fp8_max, fp8_dtype):
            return jnp.clip(t, -fp8_max, fp8_max).astype(fp8_dtype)
        key = jax.random.key(seed)
        kx, kw, kb = jax.random.split(key, 3)
        x = jax.random.normal(kx, (BATCH, SEQ, IN_FEATURES), dtype=jnp.float32)
        weight = jax.random.normal(kw, (OUT_FEATURES, IN_FEATURES), dtype=jnp.float32) * 0.02
        bias = jax.random.normal(kb, (OUT_FEATURES,), dtype=jnp.float32) * 0.02
        return {'x': x, 'weight': weight, 'bias': bias}
    _L0_ffn_in = _L0_ffn_setup()
    _d = {'L0_attn_x': _L0_attn_in['x'], 'L0_attn_w1': _L0_attn_in['w1'], 'L0_attn_w2': _L0_attn_in['w2'], 'L0_attn_b2': _L0_attn_in['b2'], 'L0_attn_sparse_mask': _L0_attn_in['sparse_mask'], 'L0_ffn_weight': _L0_ffn_in['weight'], 'L0_ffn_bias': _L0_ffn_in['bias']}
    _x0 = _d['L0_attn_x']
    _d['L0_attn_x'] = jax.random.normal(jax.random.fold_in(jax.random.key(seed), 1), (8, 512, 1024), dtype=_x0.dtype)
    del _x0
    return _d

def reference(L0_attn_x, L0_attn_w1, L0_attn_w2, L0_attn_b2, L0_attn_sparse_mask, L0_ffn_weight, L0_ffn_bias):

    def _L0_attn_ref(x, w1, w2, b2, sparse_mask):
        import math
        import jax, jax.numpy as jnp
        import numpy as np
        IN_F, OUT_F, HID = (1024, 1024, 1024)
        WINDOW, STRIPES = (6, 3)

        def make_sparse_mask(n_in=IN_F, n_out=OUT_F, window=WINDOW, stripes=STRIPES):
            m = np.zeros((n_in, n_out), dtype=np.float32)
            stride = int(math.sqrt(n_in))
            for k in range(stripes):
                ps = stride * k
                for i in range(0, n_in, window):
                    m[ps + i:ps + i + window, i:i + window] = 1.0
            mb = m.astype(bool)
            return jnp.asarray((mb | mb.T).astype(np.float32))
        attn = jnp.einsum('ds,td->st', w1, w2) * sparse_mask
        y = jnp.einsum('bds,st->bdt', x, attn) + b2
        return jax.nn.gelu(y, approximate=False)

    def _L0_ffn_ref(x, weight, bias):
        import jax, jax.numpy as jnp
        import numpy as np
        E4M3_MAX = 448.0
        E5M2_MAX = 57344.0
        EPS = 1e-12
        IN_FEATURES = 1024
        OUT_FEATURES = 1024
        BATCH, SEQ = (1, 512)

        def _amax_to_scale(amax, fp8_max):
            return fp8_max / jnp.maximum(amax, EPS)

        def _to_fp8_saturated(t, fp8_max, fp8_dtype):
            return jnp.clip(t, -fp8_max, fp8_max).astype(fp8_dtype)
        w_amax = jnp.max(jnp.abs(weight))
        w_scale = _amax_to_scale(w_amax, E4M3_MAX)
        w_q = _to_fp8_saturated(weight * w_scale, E4M3_MAX, jnp.float8_e4m3fn)
        x_amax = jnp.max(jnp.abs(x))
        x_scale = _amax_to_scale(x_amax, E5M2_MAX)
        x_q = _to_fp8_saturated(x * x_scale, E5M2_MAX, jnp.float8_e5m2)
        acc = jnp.einsum('bsk,nk->bsn', x_q.astype(jnp.float32), w_q.astype(jnp.float32))
        out = acc * (1.0 / x_scale) * (1.0 / w_scale) + bias
        return out
    x = L0_attn_x
    xn = _layernorm(x, axis=-1)
    x = x + _L0_attn_ref(xn, L0_attn_w1, L0_attn_w2, L0_attn_b2, L0_attn_sparse_mask) + _L0_ffn_ref(xn, L0_ffn_weight, L0_ffn_bias)
    return x

_drawn_inputs = setup_inputs


def setup_inputs(seed=0):
    import zlib

    import numpy as np

    out = dict(_drawn_inputs(seed))
    spreads = {}
    factors = {'L0_attn_b2': 4.58, 'L0_ffn_bias': 3.428}
    for name, (base, spread) in spreads.items():
        noise = np.random.default_rng([zlib.crc32(name.encode()), seed]).standard_normal(out[name].shape)
        drawn = base * np.exp(spread * noise) if base else spread * noise
        out[name] = jnp.asarray(drawn.astype(out[name].dtype))
    for name, factor in factors.items():
        out[name] = (out[name] * factor).astype(out[name].dtype)
    return out
```

```python
from contextlib import ExitStack

import concourse.bass as bass
from concourse import mybir

ALU = mybir.AluOpType
ACT = mybir.ActivationFunctionType
AX_X = mybir.AxisListType.X
F32 = mybir.dt.float32
F16 = mybir.dt.float16
BF16 = mybir.dt.bfloat16
E5M2 = mybir.dt.float8e5
U32 = mybir.dt.uint32
I32 = mybir.dt.int32
RMAX = bass.bass_isa.ReduceOp.max
RADD = bass.bass_isa.ReduceOp.add

P = 128
D = 1024
KB = D // P
HALF = 512

WINDOW, STRIPES = 6, 3
REACH = 32 * (STRIPES - 1) + WINDOW - 1
C0 = [max(0, P * b - REACH) for b in range(KB)]
C1 = [min(D, P * b + P + REACH) for b in range(KB)]
OFF = [sum(C1[a] - C0[a] for a in range(b)) for b in range(KB + 1)]
BAND = OFF[KB]

LN_EPS = 1e-5
AMAX_EPS = 1e-12
E4M3_MAX, E5M2_MAX = 448.0, 57344.0
XSCALE = 1024.0
ASCALE = 32768.0
A_TINY = 1e-20
E4M3_LOW = 2.0 ** -6
ROUND4 = 1.5 * 2.0 ** 20
EXP_BITS = 0x7F800000

A_AT = 4
SG = 4
ACT_SUMS = (0, 1)


def sparse_linear_plus_fp8_linear(
    nc: bass.Bass,
    x: bass.AP,
    w1: bass.AP,
    w2: bass.AP,
    b2: bass.AP,
    mask: bass.AP,
    weight: bass.AP,
    bias: bass.AP,
    out: bass.AP,
):
    x_rows = x.rearrange("b s d -> (b s) d").rearrange("(n p) d -> n p d", p=P)
    out_rows = out.rearrange("b s d -> (b s) d").rearrange("(n p) d -> n p d", p=P)
    NT = x_rows.shape[0]
    NG = NT // SG
    w1_rows = w1.rearrange("(n p) d -> n p d", p=P)
    w2_rows = w2.rearrange("(n p) d -> n p d", p=P)
    weight_rows = weight.rearrange("(n p) d -> n p d", p=P)
    mask_rows = mask.rearrange("(n p) d -> n p d", p=P)
    mask_pieces = mask.rearrange("r (h t) -> (r h) t", h=2).rearrange("(n p) t -> n p t", p=P)
    NM = mask_pieces.shape[0]
    assert NM == NT // 2 and NT % SG == 0

    with ExitStack() as ctx:
        def sb(name, shape, dt):
            return ctx.enter_context(nc.sbuf_tensor(name, shape, dt))

        def psum(name, shape, dt):
            return ctx.enter_context(nc.psum_tensor(name, shape, dt))

        def sem(name):
            return ctx.enter_context(nc.semaphore(name))

        x_all = sb("x_all", [P, NT, D], F32)
        w2_nat = x_all[:, 0:KB, :]
        w_raw = x_all[:, KB:2 * KB, :]
        w1_sb = x_all[:, 2 * KB:3 * KB, :]
        w2T = x_all[:, 3 * KB:4 * KB, :]
        xs = sb("xs", [P, 2, D], F32)
        expo = xs
        xhT = sb("xhT", [P, 2, D], F16)
        xlT = sb("xlT", [P, 2, D], F16)
        xqT = sb("xqT", [P, 2, D], E5M2)
        junk = xqT[:, :, :].rearrange("p a d -> p (a d)").bitcast(F16)
        t1 = sb("t1", [P, 2, D], F32)
        band = t1[:, :, :].rearrange("p a d -> p (a d)")[:, 0:BAND]
        res = sb("res", [P, 2, D], F32)
        sq_more = sb("sq_more", [P, 2, D], F32)
        sq = [t[:, i, :] for t in (res, sq_more) for i in range(2)]
        mask_piece = sb("mask_piece", [P, HALF], F32)
        mask_flags = sb("mask_flags", [P, HALF], BF16)
        Ah = sb("Ah", [P, BAND], F16)
        Al = sb("Al", [P, BAND], F16)
        wqT = sb("wqT", [P, KB, D], BF16)
        b2_bc = sb("b2_bc", [P, D], F32)
        bias_bc = sb("bias_bc", [P, D], F32)
        wq_nat = [xhT[:, 0, :].bitcast(BF16), xhT[:, 1, :].bitcast(BF16),
                  xlT[:, 0, :].bitcast(BF16), xlT[:, 1, :].bitcast(BF16),
                  b2_bc[:, 0:HALF].bitcast(BF16), b2_bc[:, HALF:D].bitcast(BF16),
                  bias_bc[:, 0:HALF].bitcast(BF16), bias_bc[:, HALF:D].bitcast(BF16)]
        identF = sb("identF", [P, P], F32)
        identB = sb("identB", [P, P], BF16)
        minus_half = sb("minus_half", [P, SG], F32)
        plus_half = sb("plus_half", [P, 1], F32)
        neg_mean = sb("neg_mean", [P, NT], F32)
        ssq = sb("ssq", [P, NT], F32)
        var_s = sb("var_s", [P, NT], F32)
        rs = sb("rs", [P, NT], F32)
        nb = sb("nb", [P, NT], F32)
        maxsq = sb("maxsq", [P, NT], F32)
        m2a = sb("m2a", [P, NT], F32)
        m2 = sb("m2", [P, NT], F32)
        bn = sb("bn", [P, 2, 2, 6], F32)
        mv = sb("mv", [P, 2, 2], F32)
        wmax = sb("wmax", [P, KB], F32)
        amax2 = sb("amax2", [P, 2], F32)
        sc = sb("sc", [P, 24], F32)
        (w_pm, w_am, inv_ws, ws, a_pm, a_am, a_inv, a_mul, y_mul, x_pm, x_am, x_sq, x_inv, x_mul,
         f_mul, band_cnt, all_cnt, new_cnt, off_cnt, off_any) = [sc[:, i:i + 1] for i in range(20)]
        flag = sb("flag", [P, 1], I32)

        psT = psum("psT", [P, D], F32)
        psY = psum("psY", [P, D], F32)
        psF = psum("psF", [P, D], F32)
        psZ = psum("psZ", [P, D], F32)
        psW = psT[:, 0:HALF].bitcast(BF16)
        psA = [ps[:, at:at + C1[b] - C0[b]] for b, (ps, at) in enumerate(
            [(psY, 0), (psY, HALF), (psF, 0), (psF, HALF), (psZ, 0), (psZ, HALF), (psT, HALF),
             (psY, C1[0] - C0[0])])]
        ps_y = (psY, psZ)

        const_ready = sem("const_ready")
        const_zero = sem("const_zero")
        weight_loaded = [sem(f"weight_loaded{j}") for j in range(KB)]
        w2_loaded = [sem(f"w2_loaded{j}") for j in range(KB)]
        w1_loaded = [sem(f"w1_loaded{j}") for j in range(KB)]
        band_loaded = sem("band_loaded")
        biases_loaded = sem("biases_loaded")
        x_loaded = [sem(f"x_loaded{j}") for j in range(SG)]
        w_rowmax = sem("w_rowmax")
        w_amax = sem("w_amax")
        w_scale = sem("w_scale")
        w_scaled = sem("w_scaled")
        expo_ready = sem("expo_ready")
        expo_step = sem("expo_step")
        w_summed = sem("w_summed")
        w_rounded = sem("w_rounded")
        wq_transposed = sem("wq_transposed")
        wq_copied = sem("wq_copied")
        w2_transposed = sem("w2_transposed")
        w2_copied_a = sem("w2_copied_a")
        w2_copied_v = sem("w2_copied_v")
        a_done = sem("a_done")
        a_masked = sem("a_masked")
        band_counted = sem("band_counted")
        a_rowmax = sem("a_rowmax")
        a_amax = sem("a_amax")
        a_scale = sem("a_scale")
        a_high = sem("a_high")
        a_split = sem("a_split")
        mean_a = sem("mean_a")
        mean_v = sem("mean_v")
        bn_step = sem("bn_step")
        squared = sem("squared")
        row_max = sem("row_max")
        var_ready = sem("var_ready")
        stat_step = sem("stat_step")
        x_rowmax = sem("x_rowmax")
        x_amax = sem("x_amax")
        x_scale = sem("x_scale")
        v_chain = sem("v_chain")
        g_chain = sem("g_chain")
        xs_ready = sem("xs_ready")
        x_transposed = sem("x_transposed")
        xh_ready = sem("xh_ready")
        xl_ready = sem("xl_ready")
        xq_ready = sem("xq_ready")
        y_done = sem("y_done")
        f_done = sem("f_done")
        t1_ready = sem("t1_ready")
        gelu_ready = sem("gelu_ready")
        res_ready = sem("res_ready")
        u_ready = sem("u_ready")
        out_ready = sem("out_ready")
        stored = [sem(f"stored{i}") for i in range(2)]
        mask_loaded = sem("mask_loaded")
        mask_counted = sem("mask_counted")
        cnt_added = sem("cnt_added")
        ssq_v = sem("ssq_v")
        off_ready = sem("off_ready")
        off_reduced = sem("off_reduced")
        flag_ready = sem("flag_ready")
        g_loaded = sem("g_loaded")
        g_w2_transposed = sem("g_w2_transposed")
        g_w2_copied = sem("g_w2_copied")
        g_w1_copied = sem("g_w1_copied")
        g_mask_loaded = sem("g_mask_loaded")
        g_attn_done = sem("g_attn_done")
        g_attn_masked = sem("g_attn_masked")
        g_x_loaded = sem("g_x_loaded")
        g_xs_ready = sem("g_xs_ready")
        g_x_transposed = sem("g_x_transposed")
        g_xq_ready = sem("g_xq_ready")
        g_xT_ready = sem("g_xT_ready")
        g_products_done = sem("g_products_done")
        g_t1_ready = sem("g_t1_ready")
        g_gelu_ready = sem("g_gelu_ready")
        g_sum = sem("g_sum")
        g_stored = sem("g_stored")

        attn_full = x_all[:, 0:KB, :]
        w2_slot = x_all[:, 0, :]
        x_slot = x_all[:, KB, :]
        w1_cols, xT_full = xs[:, 0, :], xs[:, 1, :]
        mask_slot = res[:, 1, :]

        block = ctx.enter_context(nc.Block())

        def when_mask_leaves_band(eng):
            eng.wait_ge(flag_ready, 1)
            return eng.If(eng.value_load(flag[0:1, 0:1], min_val=0, max_val=1))

        def over_tiles(eng, period):
            period(0, 0, 0)
            period(1, 0, 1)
            with eng.Fori(1, NT // 2 - 1) as m:
                for j in range(2):
                    period(2 * m + j, m, j)
            period(NT - 2, NT // 2 - 1, 0)
            period(NT - 1, NT // 2 - 1, 1)

        def first(q):
            return isinstance(q, int) and q < 2

        def last(q):
            return isinstance(q, int) and q == NT - 1

        @block.sync
        def _(sp):
            for j in range(KB):
                sp.dma_start(w_raw[:, j, :], weight_rows[j]).then_inc(weight_loaded[j], 16)
            for j in range(KB):
                sp.dma_start(w2_nat[:, j, :], w2_rows[j]).then_inc(w2_loaded[j], 16)
            def load_x(g, j):
                if not isinstance(g, int) or g > 0:
                    sp.wait_ge(x_loaded[j], 16 * g)
                sp.dma_start(x_all[:, SG * g + j, :], x_rows[SG * g + j]).then_inc(x_loaded[j], 16)

            for i in range(KB):
                sp.wait_ge(w2_transposed, i + 1)
                load_x(i // SG, i % SG)
            for j in range(KB):
                sp.dma_start(w1_sb[:, j, :], w1_rows[j]).then_inc(w1_loaded[j], 16)
            for b in range(KB):
                sp.dma_start(band[:, OFF[b]:OFF[b + 1]], mask_rows[b, :, C0[b]:C1[b]])\
                    .then_inc(band_loaded, 16)
            for i in range(KB):
                sp.wait_ge(w_rounded, i + 1)
                load_x((KB + i) // SG, i % SG)
            sp.wait_ge(a_done, 1)
            with sp.Fori(2 * KB // SG, NG) as g:
                for j in range(SG):
                    load_x(g, j)
            sp.wait_ge(wq_transposed, KB)
            sp.dma_start(b2_bc[:, :], b2.partition_broadcast(P)).then_inc(biases_loaded, 16)
            sp.dma_start(bias_bc[:, :], bias.partition_broadcast(P)).then_inc(biases_loaded, 16)

            def period(q, m, par):
                if par == 0:
                    if not first(q):
                        sp.wait_ge(mask_counted, m)
                    sp.dma_start(mask_piece[:, :], mask_pieces[m]).then_inc(mask_loaded, 16)
                sp.wait_ge(out_ready, q + 1)
                sp.dma_start(out_rows[q], t1[:, par, :]).then_inc(stored[par], 16)

            over_tiles(sp, period)
            for par in range(2):
                sp.wait_ge(stored[par], 16 * (NT // 2))

            def turns(n, turn):
                turn(0)
                with sp.Fori(1, n) as i:
                    turn(i)

            def later(i, signal, value):
                if not isinstance(i, int):
                    sp.wait_ge(signal, value)

            def weights(j):
                later(j, g_w2_copied, j)
                sp.dma_start(w1_sb[:, j, :], w1_rows[j]).then_inc(g_loaded, 16)
                sp.dma_start(w2_slot, w2_rows[j]).then_inc(g_loaded, 16)

            def mask_block(b):
                later(b, g_attn_masked, b)
                sp.dma_start(mask_slot, mask_rows[b]).then_inc(g_mask_loaded, 16)

            def tile(t):
                later(t, g_stored, 16 * t)
                sp.dma_start(x_slot, x_rows[t]).then_inc(g_x_loaded, 16)
                sp.wait_ge(g_sum, 3 * t + 3)
                sp.dma_start(out_rows[t], res[:, 0, :]).then_inc(g_stored, 16)

            with when_mask_leaves_band(sp):
                turns(KB, weights)
                turns(KB, mask_block)
                turns(NT, tile)
                sp.wait_ge(g_stored, 16 * NT)

        @block.gpsimd
        def _(pool):
            chain = [0]

            def then(ins):
                chain[0] += 1
                ins.then_inc(g_chain, 1)
                pool.wait_ge(g_chain, chain[0])

            nc.gpsimd.memset(identF[:, :], 0.0).then_inc(const_zero, 1)
            nc.gpsimd.memset(identB[:, :], 0.0).then_inc(const_zero, 1)
            nc.gpsimd.memset(minus_half[:, :], -0.5).then_inc(const_ready, 1)
            nc.gpsimd.memset(plus_half[:, :], 0.5).then_inc(const_ready, 1)
            pool.wait_ge(const_zero, 2)
            for m in (identF, identB):
                nc.gpsimd.affine_select(out=m[:, :], in_=m[:, :], compare_op=ALU.not_equal, fill=1.0,
                                        base=0, pattern=[[-1, P]], channel_multiplier=1)\
                    .then_inc(const_ready, 1)
            pool.wait_ge(const_ready, 4)

            pool.wait_ge(w_rowmax, 1)
            nc.gpsimd.partition_all_reduce(w_am, w_pm, P, RMAX).then_inc(w_amax, 1)

            for j in range(KB):
                pool.wait_ge(expo_ready, j + 1)
                pool.wait_ge(w_scaled, j + 1)
                nc.gpsimd.tensor_tensor(w_raw[:, j, :], w_raw[:, j, :], expo[:, j % 2, :], ALU.add)\
                    .then_inc(w_summed, 1)
                pool.wait_ge(w_summed, j + 1)
                nc.gpsimd.tensor_tensor(wq_nat[j], w_raw[:, j, :], expo[:, j % 2, :],
                                        ALU.subtract).then_inc(w_rounded, 1)

            def step(g):
                cols = bass.ds(SG * g, SG)
                pool.wait_ge(var_ready, g + 1)
                nc.gpsimd.tensor_tensor(rs[:, cols], var_s[:, cols], minus_half[:, :], ALU.pow)\
                    .then_inc(stat_step, 1)
                pool.wait_ge(stat_step, 4 * g + 1)
                nc.gpsimd.tensor_tensor(nb[:, cols], neg_mean[:, cols], rs[:, cols], ALU.mult)\
                    .then_inc(stat_step, 1)
                pool.wait_ge(row_max, SG * g + SG)
                nc.gpsimd.tensor_tensor(m2a[:, cols], maxsq[:, cols], rs[:, cols], ALU.mult)\
                    .then_inc(stat_step, 1)
                pool.wait_ge(stat_step, 4 * g + 3)
                nc.gpsimd.tensor_tensor(m2[:, cols], m2a[:, cols], rs[:, cols], ALU.mult)\
                    .then_inc(stat_step, 1)

            with pool.Fori(0, A_AT) as g:
                step(g)
            pool.wait_ge(a_rowmax, 1)
            nc.gpsimd.partition_all_reduce(a_am, a_pm, P, RMAX).then_inc(a_amax, 1)
            with pool.Fori(A_AT, NG) as g:
                step(g)
            pool.wait_ge(x_rowmax, 1)
            then(nc.gpsimd.partition_all_reduce(x_sq, x_pm, P, RMAX))
            nc.gpsimd.tensor_tensor(x_am, x_sq, plus_half[:, :], ALU.pow).then_inc(x_amax, 1)

            def residual(q, m, par):
                if not first(q):
                    pool.wait_ge(out_ready, q - 1)
                nc.gpsimd.tensor_tensor(res[:, par, :], x_all[:, q, :], bias_bc[:, :], ALU.add)\
                    .then_inc(res_ready, 1)

            def period(q, m, par):
                if not last(q):
                    if par == 0:
                        residual(q + 1, m, 1)
                    else:
                        residual(q + 1, m + 1, 0)
                pool.wait_ge(gelu_ready, q + 1)
                pool.wait_ge(res_ready, q + 1)
                nc.gpsimd.tensor_tensor(res[:, par, :], res[:, par, :], t1[:, par, :], ALU.add)\
                    .then_inc(u_ready, 1)

            pool.wait_ge(biases_loaded, 32)
            residual(0, 0, 0)
            over_tiles(pool, period)
            pool.wait_ge(off_ready, 1)
            nc.gpsimd.partition_all_reduce(off_any, off_cnt, P, RADD).then_inc(off_reduced, 1)

        @block.scalar
        def _(act):
            act.preload_act_table(ACT.Gelu)

            def copy_w2(j):
                act.wait_ge(w2_transposed, j + 1)
                act.activation(w2T[:, :, P * j:P * j + P],
                               (psT, psZ)[j % 2][:, :].rearrange("p (k t) -> p k t", k=KB),
                               ACT.Copy).then_inc(w2_copied_a, 1)

            def scale_w(j):
                act.activation(w_raw[:, j, :], w_raw[:, j, :], ACT.Copy, scale=ws).then_inc(w_scaled, 1)

            def copy_wq(j):
                act.wait_ge(wq_transposed, j + 1)
                act.activation(wqT[:, :, P * j:P * j + P],
                               psW.rearrange("p (k t) -> p k t", k=KB),
                               ACT.Copy).then_inc(wq_copied, 1)

            act.wait_ge(w_scale, 1)
            for j in range(KB):
                scale_w(j)
                if j % 2 == 0:
                    copy_w2(j)

            def step(g):
                for j in range(SG):
                    i = SG * g + j
                    col = bass.ds(i, 1)
                    if j in ACT_SUMS:
                        n = len(ACT_SUMS) * g + ACT_SUMS.index(j) + 1
                        act.wait_ge(x_loaded[j], 16 * (g + 1))
                        if not (isinstance(g, int) and g == 0 and j == 0):
                            act.wait_ge(squared, i)
                        act.activation(junk, x_all[:, i, :], ACT.Copy, scale=-1.0 / D,
                                       accum_out=neg_mean[:, col]).then_inc(mean_a, 1)
                        act.wait_ge(mean_a, n)
                    else:
                        n = (SG - len(ACT_SUMS)) * g + j - len(ACT_SUMS) + 1
                        act.wait_ge(mean_v, n)
                        act.wait_ge(x_loaded[j], 16 * (g + 1))
                    if not (isinstance(g, int) and g == 0):
                        act.wait_ge(row_max, i - SG + 1)
                    if j in ACT_SUMS:
                        act.activation(sq[j], x_all[:, i, :], ACT.Square,
                                       bias=neg_mean[:, col], accum_out=ssq[:, col]).then_inc(squared, 1)
                    else:
                        act.activation(sq[j], x_all[:, i, :], ACT.Square,
                                       bias=neg_mean[:, col]).then_inc(squared, 1)

            step(0)
            with act.Fori(1, A_AT) as g:
                step(g)
            for j in range(KB):
                copy_wq(j)
            with act.Fori(A_AT, NG) as g:
                step(g)

            def normalise(q, par):
                if not first(q):
                    act.wait_ge(x_transposed, q - 1)
                act.activation(xs[:, par, :], x_all[:, q, :], ACT.Identity,
                               scale=rs[:, bass.ds(q, 1)], bias=nb[:, bass.ds(q, 1)]).then_inc(xs_ready, 1)

            def high(q, par):
                act.wait_ge(x_transposed, q + 1)
                if not first(q):
                    act.wait_ge(y_done, q - 1)
                    act.wait_ge(f_done, q - 1)
                act.activation(xhT[:, par, :], psT[:, :], ACT.Copy).then_inc(xh_ready, 1)

            def quantise(q, par):
                act.activation(xqT[:, par, :], psT[:, :], ACT.Copy, scale=x_mul, saturate=False)\
                    .then_inc(xq_ready, 1)

            act.wait_ge(stat_step, 4 * NG)
            act.wait_ge(w_rounded, KB)
            act.wait_ge(wq_transposed, KB)
            normalise(0, 0)
            normalise(1, 1)
            act.wait_ge(x_scale, 1)
            high(0, 0)
            quantise(0, 0)

            def period(q, m, par):
                if not last(q):
                    high(q + 1, 1 - par)
                    quantise(q + 1, 1 - par)
                if not (isinstance(q, int) and q >= NT - 2):
                    normalise(q + 2, par)
                act.wait_ge(t1_ready, q + 1)
                act.activation(t1[:, par, :], t1[:, par, :], ACT.Gelu).then_inc(gelu_ready, 1)

            over_tiles(act, period)

            with when_mask_leaves_band(act):
                with act.Fori(0, KB) as j:
                    act.wait_ge(g_w2_transposed, j + 1)
                    act.activation(w2T[:, :, bass.ds(P * j, P)],
                                   psT[:, :].rearrange("p (k t) -> p k t", k=KB), ACT.Copy)\
                        .then_inc(g_w2_copied, 1)
                act.wait_ge(g_loaded, 32 * KB)
                with act.Fori(0, KB) as b:
                    act.activation(w1_cols.rearrange("p (k s) -> p k s", k=KB),
                                   w1_sb[:, :, bass.ds(P * b, P)], ACT.Copy).then_inc(g_w1_copied, 1)
                    act.wait_ge(g_attn_masked, b + 1)
                with act.Fori(0, NT) as t:
                    act.wait_ge(g_x_loaded, 16 * t + 16)
                    act.activation(xs[:, 0, :], x_slot, ACT.Identity, scale=rs[:, bass.ds(t, 1)],
                                   bias=nb[:, bass.ds(t, 1)]).then_inc(g_xs_ready, 1)
                    act.wait_ge(g_x_transposed, t + 1)
                    act.activation(xT_full, psT[:, :], ACT.Copy).then_inc(g_xT_ready, 1)
                    act.activation(xqT[:, 0, :], psT[:, :], ACT.Copy, scale=x_mul, saturate=False)\
                        .then_inc(g_xq_ready, 1)
                    act.wait_ge(g_t1_ready, t + 1)
                    act.activation(t1[:, 0, :], t1[:, 0, :], ACT.Gelu).then_inc(g_gelu_ready, 1)

        @block.vector
        def _(dve):
            chain = [0]

            def then(ins):
                chain[0] += 1
                ins.then_inc(v_chain, 1)
                dve.wait_ge(v_chain, chain[0])

            for j in range(KB):
                dve.wait_ge(weight_loaded[j], 16)
                ins = nc.vector.tensor_reduce(wmax[:, j:j + 1], w_raw[:, j, :], AX_X, ALU.max,
                                              apply_absolute_value=True)
            then(ins)
            nc.vector.tensor_reduce(w_pm, wmax[:, :], AX_X, ALU.max).then_inc(w_rowmax, 1)
            dve.wait_ge(w_amax, 1)
            then(nc.vector.tensor_scalar(inv_ws, w_am, AMAX_EPS, 1.0 / E4M3_MAX, ALU.max, ALU.mult))
            nc.vector.reciprocal(ws, inv_ws).then_inc(w_scale, 1)

            def exponent(j):
                dve.wait_ge(w_scaled, j + 1)
                if j >= 2:
                    dve.wait_ge(w_rounded, j - 1)
                nc.vector.tensor_scalar(expo[:, j % 2, :].bitcast(U32), w_raw[:, j, :].bitcast(U32),
                                        EXP_BITS, None, ALU.bitwise_and).then_inc(expo_step, 1)
                dve.wait_ge(expo_step, j + 1)
                nc.vector.tensor_scalar(expo[:, j % 2, :], expo[:, j % 2, :], E4M3_LOW, ROUND4,
                                        ALU.max, ALU.mult).then_inc(expo_ready, 1)

            exponent(0)
            exponent(1)
            exponent(2)
            for j in range(1, KB, 2):
                dve.wait_ge(w2_transposed, j + 1)
                nc.vector.tensor_copy(w2T[:, :, P * j:P * j + P],
                                      psZ[:, :].rearrange("p (k t) -> p k t", k=KB))\
                    .then_inc(w2_copied_v, 1)
            NV = SG - len(ACT_SUMS)

            def step(g):
                def sums(j):
                    dve.wait_ge(x_loaded[j], 16 * (g + 1))
                    for h in range(2):
                        nc.vector.bn_stats(bn[:, j % 2, h, :],
                                           x_all[:, SG * g + j, HALF * h:HALF * h + HALF])\
                            .then_inc(bn_step, 1)

                def mean(j):
                    i = SG * g + j
                    nc.vector.bn_aggr(mv[:, j % 2, :], bn[:, j % 2, :, :].rearrange("p a b -> p (a b)"))\
                        .then_inc(bn_step, 1)
                    dve.wait_ge(bn_step, 3 * NV * g + 2 * NV + j - len(ACT_SUMS) + 1)
                    nc.vector.tensor_scalar(neg_mean[:, bass.ds(i, 1)], mv[:, j % 2, 0:1], -1.0, None,
                                            ALU.mult).then_inc(mean_v, 1)
                    nc.vector.tensor_scalar(ssq[:, bass.ds(i, 1)], mv[:, j % 2, 1:2], float(D), None,
                                            ALU.mult).then_inc(ssq_v, 1)

                def maximum(j):
                    i = SG * g + j
                    dve.wait_ge(squared, i + 1)
                    nc.vector.tensor_reduce(maxsq[:, bass.ds(i, 1)], sq[j], AX_X, ALU.max)\
                        .then_inc(row_max, 1)

                for j in range(len(ACT_SUMS), SG):
                    sums(j)
                dve.wait_ge(bn_step, 3 * NV * g + 2 * NV)
                maximum(0)
                for j in range(len(ACT_SUMS), SG):
                    mean(j)
                for j in range(1, SG):
                    maximum(j)
                dve.wait_ge(ssq_v, NV * (g + 1))
                nc.vector.tensor_scalar(var_s[:, bass.ds(SG * g, SG)], ssq[:, bass.ds(SG * g, SG)],
                                        1.0 / D / XSCALE ** 2, LN_EPS / XSCALE ** 2,
                                        ALU.mult, ALU.add).then_inc(var_ready, 1)

            step(0)
            exponent(3)
            exponent(4)
            step(1)
            for j in range(5, KB):
                exponent(j)
            with dve.Fori(2, A_AT) as g:
                step(g)

            dve.wait_ge(band_loaded, 16 * KB)
            nc.vector.tensor_scalar(Ah[:, :], band, 0.0, None, ALU.not_equal, ALU.add,
                                    accum_out=band_cnt).then_inc(band_counted, 1)
            dve.wait_ge(band_counted, 1)
            dve.wait_ge(a_done, 1)
            for b in range(KB):
                nc.vector.tensor_tensor(band[:, OFF[b]:OFF[b + 1]], psA[b], band[:, OFF[b]:OFF[b + 1]],
                                        ALU.mult).then_inc(a_masked, 1)
            dve.wait_ge(a_masked, KB)
            nc.vector.tensor_reduce(a_pm, band, AX_X, ALU.max, apply_absolute_value=True).then_inc(a_rowmax, 1)
            dve.wait_ge(a_amax, 1)
            then(nc.vector.tensor_scalar(a_inv, a_am, A_TINY, 1.0 / ASCALE, ALU.max, ALU.mult))
            then(nc.vector.reciprocal(a_mul, a_inv))
            nc.vector.tensor_scalar(y_mul, a_inv, 1.0 / XSCALE, None, ALU.mult).then_inc(a_scale, 1)
            nc.vector.tensor_scalar(Ah[:, :], band, a_mul, None, ALU.mult).then_inc(a_high, 1)
            dve.wait_ge(a_high, 1)
            nc.vector.scalar_tensor_tensor(out=Al[:, :], in0=band, scalar=a_mul, in1=Ah[:, :],
                                           op0=ALU.mult, op1=ALU.subtract).then_inc(a_split, 1)

            with dve.Fori(A_AT, NG) as g:
                step(g)

            dve.wait_ge(stat_step, 4 * NG)
            nc.vector.tensor_reduce(x_pm, m2[:, :], AX_X, ALU.max).then_inc(x_rowmax, 1)
            dve.wait_ge(x_amax, 1)
            then(nc.vector.tensor_scalar(x_inv, x_am, XSCALE * AMAX_EPS, 1.0 / E5M2_MAX, ALU.max, ALU.mult))
            then(nc.vector.tensor_scalar(f_mul, x_inv, inv_ws, 1.0 / XSCALE, ALU.mult, ALU.mult))
            nc.vector.reciprocal(x_mul, x_inv).then_inc(x_scale, 1)
            dve.wait_ge(biases_loaded, 32)
            dve.wait_ge(a_split, 1)

            def low(q, par):
                dve.wait_ge(xq_ready, q + 1)
                if not first(q):
                    dve.wait_ge(y_done, q - 1)
                nc.vector.tensor_tensor(xlT[:, par, :], psT[:, :], xhT[:, par, :], ALU.subtract)\
                    .then_inc(xl_ready, 1)

            def finish(q, par):
                dve.wait_ge(f_done, q + 1)
                dve.wait_ge(u_ready, q + 1)
                nc.vector.scalar_tensor_tensor(out=t1[:, par, :], in0=psF[:, :], scalar=f_mul,
                                               in1=res[:, par, :], op0=ALU.mult, op1=ALU.add)\
                    .then_inc(out_ready, 1)

            def count_mask(m):
                dve.wait_ge(mask_loaded, 16 * (m + 1))
                if isinstance(m, int) and m == 0:
                    nc.vector.tensor_scalar(mask_flags[:, :], mask_piece[:, :], 0.0, None, ALU.not_equal,
                                            ALU.add, accum_out=all_cnt).then_inc(mask_counted, 1)
                else:
                    dve.wait_ge(mask_counted, m)
                    dve.wait_ge(cnt_added, m)
                    nc.vector.tensor_scalar(mask_flags[:, :], mask_piece[:, :], 0.0, None, ALU.not_equal,
                                            ALU.add, accum_out=new_cnt).then_inc(mask_counted, 1)
                    dve.wait_ge(mask_counted, m + 1)
                    nc.vector.tensor_tensor(all_cnt, all_cnt, new_cnt, ALU.add)\
                        .then_inc(cnt_added, 1)

            def period(q, m, par):
                if not (isinstance(q, int) and q == 0):
                    finish(q - 1, 1 - par)
                if not last(q):
                    low(q + 1, 1 - par)
                dve.wait_ge(y_done, q + 1)
                if not first(q):
                    dve.wait_ge(stored[par], 16 * m)
                nc.vector.scalar_tensor_tensor(out=t1[:, par, :], in0=ps_y[par][:, :], scalar=y_mul,
                                               in1=b2_bc[:, :], op0=ALU.mult, op1=ALU.add)\
                    .then_inc(t1_ready, 1)
                if par == 1:
                    count_mask(m)

            low(0, 0)
            nc.vector.memset(new_cnt, 0.0).then_inc(cnt_added, 1)
            over_tiles(dve, period)
            finish(NT - 1, 1)
            dve.wait_ge(cnt_added, NM)
            nc.vector.tensor_tensor(off_cnt, all_cnt, band_cnt, ALU.subtract).then_inc(off_ready, 1)
            dve.wait_ge(off_reduced, 1)
            nc.vector.tensor_scalar(flag[:, :], off_any, 0.5, None, ALU.is_gt).then_inc(flag_ready, 1)

            with when_mask_leaves_band(dve):
                with dve.Fori(0, KB) as b:
                    dve.wait_ge(g_attn_done, b + 1)
                    dve.wait_ge(g_mask_loaded, 16 * b + 16)
                    nc.vector.tensor_tensor(attn_full[:, b, :], psY[:, :], mask_slot, ALU.mult)\
                        .then_inc(g_attn_masked, 1)
                with dve.Fori(0, NT) as t:
                    dve.wait_ge(g_products_done, t + 1)
                    nc.vector.scalar_tensor_tensor(out=t1[:, 0, :], in0=psY[:, :], scalar=1.0 / XSCALE,
                                                   in1=b2_bc[:, :], op0=ALU.mult, op1=ALU.add)\
                        .then_inc(g_t1_ready, 1)
                    nc.vector.tensor_tensor(res[:, 0, :], x_slot, bias_bc[:, :], ALU.add)\
                        .then_inc(g_sum, 1)
                    dve.wait_ge(g_sum, 3 * t + 1)
                    dve.wait_ge(g_gelu_ready, t + 1)
                    nc.vector.tensor_tensor(res[:, 0, :], res[:, 0, :], t1[:, 0, :], ALU.add)\
                        .then_inc(g_sum, 1)
                    dve.wait_ge(g_sum, 3 * t + 2)
                    nc.vector.scalar_tensor_tensor(out=res[:, 0, :], in0=psF[:, :], scalar=f_mul,
                                                   in1=res[:, 0, :], op0=ALU.mult, op1=ALU.add)\
                        .then_inc(g_sum, 1)

        @block.tensor
        def _(pe):
            pe.wait_ge(const_ready, 4)
            for j in range(KB):
                pe.wait_ge(w2_loaded[j], 16)
                if j >= 2:
                    pe.wait_ge((w2_copied_a, w2_copied_v)[j % 2], j // 2)
                for k in range(KB):
                    ins = nc.tensor.transpose((psT, psZ)[j % 2][:, P * k:P * k + P],
                                              w2_nat[:, j, P * k:P * k + P], identF[:, :])
                ins.then_inc(w2_transposed, 1)
            pe.wait_ge(w2_copied_a, KB // 2)
            pe.wait_ge(w2_copied_v, KB // 2)

            for blocks in (range(0, 4), range(4, KB)):
                for k in range(KB):
                    pe.wait_ge(w1_loaded[k], 16)
                    for b in blocks:
                        ins = nc.tensor.matmul(psA[b], w1_sb[:, k, P * b:P * b + P],
                                               w2T[:, k, C0[b]:C1[b]], start=(k == 0), stop=(k == KB - 1))
            ins.then_inc(a_done, 1)

            for j in range(KB):
                pe.wait_ge(w_rounded, j + 1)
                if j >= 1:
                    pe.wait_ge(wq_copied, j)
                for k in range(KB):
                    ins = nc.tensor.transpose(psW[:, P * k:P * k + P], wq_nat[j][:, P * k:P * k + P],
                                              identB[:, :])
                ins.then_inc(wq_transposed, 1)

            def transpose_x(q, par):
                pe.wait_ge(xs_ready, q + 1)
                if not (isinstance(q, int) and q == 0):
                    pe.wait_ge(xl_ready, q)
                for k in range(KB):
                    ins = nc.tensor.transpose(psT[:, P * k:P * k + P], xs[:, par, P * k:P * k + P],
                                              identF[:, :])
                ins.then_inc(x_transposed, 1)

            pieces = [[(b, max(C0[b], HALF * h), min(C1[b], HALF * h + HALF)) for b in range(KB)
                       if max(C0[b], HALF * h) < min(C1[b], HALF * h + HALF)] for h in range(2)]

            def attn(q, par):
                pe.wait_ge(xl_ready, q + 1)
                if not first(q):
                    pe.wait_ge(t1_ready, q - 1)
                for h in range(2):
                    todo = [(b, lo, hi, xT, A) for b, lo, hi in pieces[h]
                            for xT, A in ((xhT, Ah), (xhT, Al), (xlT, Ah))]
                    for n, (b, lo, hi, xT, A) in enumerate(todo):
                        if h == 1 and n == len(todo) - 1 and not (isinstance(q, int) and q == 0):
                            pe.wait_ge(out_ready, q)
                        at = OFF[b] + lo - C0[b]
                        ins = nc.tensor.matmul(ps_y[par][:, lo:hi], xT[:, par, P * b:P * b + P],
                                               A[:, at:at + hi - lo], start=(n == 0),
                                               stop=(n == len(todo) - 1), skip_group_check=True)
                ins.then_inc(y_done, 1)

            def ffn(q, par):
                for k in range(KB):
                    for h in range(2):
                        ins = nc.tensor.matmul(psF[:, HALF * h:HALF * h + HALF],
                                               xqT[:, par, P * k:P * k + P],
                                               wqT[:, k, HALF * h:HALF * h + HALF],
                                               start=(k == 0), stop=(k == KB - 1))
                ins.then_inc(f_done, 1)

            def period(q, m, par):
                if not last(q):
                    transpose_x(q + 1, 1 - par)
                attn(q, par)
                ffn(q, par)

            pe.wait_ge(wq_copied, KB)
            pe.wait_ge(a_masked, KB)
            pe.wait_ge(a_split, 1)
            transpose_x(0, 0)
            over_tiles(pe, period)

            with when_mask_leaves_band(pe):
                with pe.Fori(0, KB) as j:
                    pe.wait_ge(g_loaded, 32 * j + 32)
                    for k in range(KB):
                        ins = nc.tensor.transpose(psT[:, P * k:P * k + P], w2_slot[:, P * k:P * k + P],
                                                  identF[:, :])
                    ins.then_inc(g_w2_transposed, 1)
                pe.wait_ge(g_w2_copied, KB)
                with pe.Fori(0, KB) as b:
                    pe.wait_ge(g_w1_copied, b + 1)
                    for h in range(2):
                        for k in range(KB):
                            ins = nc.tensor.matmul(psY[:, HALF * h:HALF * h + HALF],
                                                   w1_cols[:, P * k:P * k + P],
                                                   w2T[:, k, HALF * h:HALF * h + HALF],
                                                   start=(k == 0), stop=(k == KB - 1))
                    ins.then_inc(g_attn_done, 1)
                with pe.Fori(0, NT) as t:
                    pe.wait_ge(g_xs_ready, t + 1)
                    for k in range(KB):
                        ins = nc.tensor.transpose(psT[:, P * k:P * k + P], xs[:, 0, P * k:P * k + P],
                                                  identF[:, :])
                    ins.then_inc(g_x_transposed, 1)
                    pe.wait_ge(g_xq_ready, t + 1)
                    for h in range(2):
                        for k in range(KB):
                            nc.tensor.matmul(psY[:, HALF * h:HALF * h + HALF],
                                             xT_full[:, P * k:P * k + P],
                                             attn_full[:, k, HALF * h:HALF * h + HALF],
                                             start=(k == 0), stop=(k == KB - 1))
                    for k in range(KB):
                        for h in range(2):
                            ins = nc.tensor.matmul(psF[:, HALF * h:HALF * h + HALF],
                                                   xqT[:, 0, P * k:P * k + P],
                                                   wqT[:, k, HALF * h:HALF * h + HALF],
                                                   start=(k == 0), stop=(k == KB - 1))
                    ins.then_inc(g_products_done, 1)


_INS = ["L0_attn_x", "L0_attn_w1", "L0_attn_w2", "L0_attn_b2", "L0_attn_sparse_mask", "L0_ffn_weight",
        "L0_ffn_bias"]
_OUTS = [((8, 512, 1024), "float32")]


def kernel(**inputs):
    import numpy as _np
    import concourse.bacc as _bacc
    from concourse import mybir as _mybir
    from concourse.bass_utils import run_bass_kernel_spmd as _run

    nc = _bacc.Bacc("TRN2", target_bir_lowering=False, num_devices=1)
    arrays, args = {}, []
    for name in _INS:
        a = _np.ascontiguousarray(inputs[name])
        arrays[f"in_{name}_dram"] = a
        args.append(nc.dram_tensor(f"in_{name}_dram", a.shape, _mybir.dt.from_np(a.dtype), kind="ExternalInput").ap())
    for i, (shape, dtype) in enumerate(_OUTS):
        dt = _mybir.dt.from_np(_np.dtype(dtype))
        args.append(nc.dram_tensor(f"out_{i}_dram", shape, dt, kind="ExternalOutput").ap())
    sparse_linear_plus_fp8_linear(nc, *args)
    r = _run(nc, [arrays], core_ids=[0])
    got = tuple(r.results[0][f"out_{i}_dram"] for i in range(len(_OUTS)))
    return got[0]
```
